# Optimizing a Trainium2 kernel written in Bass

```python
import numpy as np
import jax
import jax.numpy as jnp

def _softmax(x, axis=-1):
    return jax.nn.softmax(x, axis=axis)

def _gelu(x):
    return jax.nn.gelu(x, approximate=True)

def _silu(x):
    return jax.nn.silu(x)

def _sigmoid(x):
    return jax.nn.sigmoid(x)

def _layernorm(x, axis=-1, eps=1e-05):
    m = jnp.mean(x, axis=axis, keepdims=True)
    v = jnp.var(x, axis=axis, keepdims=True)
    return (x - m) / jnp.sqrt(v + eps)

def _scatter_add(tgt, idx, src, axis=0):
    return tgt.at[idx].add(src)

def _segment_sum(src, seg, n):
    return jax.ops.segment_sum(src, seg, n)
kernel_name = 'mk_gnn_ffn_d1_gnn_r8_071fa7'

def setup_inputs(seed: int=0):
    np.random.seed(seed)
    _w = jnp.asarray

    def _rec_inputs():
        import jax
        import jax.numpy as jnp
        _gk = jax.random.key(seed)
        x = -0.0003713 + 1 * jax.random.normal(jax.random.fold_in(_gk, 1), (6250, 256), jnp.float32)
        src = jax.random.randint(jax.random.fold_in(_gk, 2), (100000,), 0, 6250, jnp.int32)
        dst = jnp.minimum((6250 * jax.random.uniform(jax.random.fold_in(_gk, 3), (100000,)) ** 2.0).astype(jnp.int32), 49999)
        _o = jnp.argsort(dst, stable=True)
        src = src[_o]
        dst = dst[_o]
        edge_attr_96 = -4.21973e-05 + 0.999841 * jax.random.normal(jax.random.fold_in(_gk, 12), (100000, 96), jnp.float32)
        return (x, src, dst, edge_attr_96)
    x, src, dst, edge_attr_96 = _rec_inputs()

    def _L0_gnn_setup():
        import jax, jax.numpy as jnp
        import numpy as np
        N_NODES = 6250
        N_EDGES = 100000
        EDGE_F = 96
        NODE_F = 256
        GLOB_F = 64
        HIDDEN = 1024
        N_GRAPHS = 8
        MLP_IN = NODE_F + 3 * EDGE_F + GLOB_F
        key = jax.random.key(seed)
        ks = jax.random.split(key, 9)
        x = jax.random.normal(ks[0], (N_NODES, NODE_F), dtype=jnp.float32)
        edge_attr = jax.random.normal(ks[1], (N_EDGES, EDGE_F), dtype=jnp.float32)
        u = jax.random.normal(ks[2], (N_GRAPHS, GLOB_F), dtype=jnp.float32)
        W1 = jax.random.normal(ks[3], (MLP_IN, HIDDEN), dtype=jnp.float32) * (1.0 / np.sqrt(MLP_IN))
        b1 = jax.random.normal(ks[4], (HIDDEN,), dtype=jnp.float32) * 0.01
        W2 = jax.random.normal(ks[5], (HIDDEN, NODE_F), dtype=jnp.float32) * (1.0 / np.sqrt(HIDDEN))
        b2 = jax.random.normal(ks[6], (NODE_F,), dtype=jnp.float32) * 0.01
        edge_index = jax.random.randint(ks[7], (2, N_EDGES), 0, N_NODES, dtype=jnp.int64 if jax.config.jax_enable_x64 else jnp.int32)
        batch = jnp.sort(jax.random.randint(ks[8], (N_NODES,), 0, N_GRAPHS, dtype=jnp.int32))
        return {'x': x, 'edge_attr': edge_attr, 'u': u, 'W1': W1, 'b1': b1, 'W2': W2, 'b2': b2, 'edge_index': edge_index, 'batch': batch}
    _L0_gnn_all = _L0_gnn_setup()
    _L0_gnn_in = {k: v for k, v in _L0_gnn_all.items() if k in ('u', 'W1', 'b1', 'W2', 'b2')}
    del _L0_gnn_all

    def _L0_ffn_setup():
        import jax, jax.numpy as jnp
        import numpy as np
        B, S, H, F, E, K = (8, 512, 256, 512, 16, 2)
        EPS = 1e-05
        key = jax.random.key(seed)
        ks = jax.random.split(key, 9)
        sc = 0.02
        return {'x': jax.random.normal(ks[0], (B, S, H), dtype=jnp.float32), 'gate_w': jax.random.normal(ks[1], (H, E), dtype=jnp.float32) * sc, 'gate_b': jnp.zeros((E,), dtype=jnp.float32), 'w1': jax.random.normal(ks[2], (E, H, F), dtype=jnp.float32) * sc, 'b1': jnp.zeros((E, F), dtype=jnp.float32), 'w2': jax.random.normal(ks[3], (E, F, H), dtype=jnp.float32) * sc, 'b2': jnp.zeros((E, H), dtype=jnp.float32), 'gamma': jnp.ones((H,), dtype=jnp.float32), 'beta': jnp.zeros((H,), dtype=jnp.float32)}
    _L0_ffn_all = _L0_ffn_setup()
    _L0_ffn_in = {k: v for k, v in _L0_ffn_all.items() if k in ('gate_w', 'gate_b', 'w1', 'b1', 'w2', 'b2', 'gamma', 'beta')}
    del _L0_ffn_all
    return {'x': x, 'src': src, 'dst': dst, 'edge_attr_96': edge_attr_96, 'L0_gnn_u': _L0_gnn_in['u'], 'L0_gnn_W1': _L0_gnn_in['W1'], 'L0_gnn_b1': _L0_gnn_in['b1'], 'L0_gnn_W2': _L0_gnn_in['W2'], 'L0_gnn_b2': _L0_gnn_in['b2'], 'L0_ffn_gate_w': _L0_ffn_in['gate_w'], 'L0_ffn_gate_b': _L0_ffn_in['gate_b'], 'L0_ffn_w1': _L0_ffn_in['w1'], 'L0_ffn_b1': _L0_ffn_in['b1'], 'L0_ffn_w2': _L0_ffn_in['w2'], 'L0_ffn_b2': _L0_ffn_in['b2'], 'L0_ffn_gamma': _L0_ffn_in['gamma'], 'L0_ffn_beta': _L0_ffn_in['beta']}

def reference(x, src, dst, edge_attr_96, L0_gnn_u, L0_gnn_W1, L0_gnn_b1, L0_gnn_W2, L0_gnn_b2, L0_ffn_gate_w, L0_ffn_gate_b, L0_ffn_w1, L0_ffn_b1, L0_ffn_w2, L0_ffn_b2, L0_ffn_gamma, L0_ffn_beta):
    import jax
    import jax.numpy as jnp

    def _L0_gnn_ref(x, edge_attr, u, W1, b1, W2, b2, edge_index, batch):
        import jax, jax.numpy as jnp
        import numpy as np
        N_NODES = 6250
        N_EDGES = 100000
        EDGE_F = 96
        NODE_F = 256
        GLOB_F = 64
        HIDDEN = 1024
        N_GRAPHS = 8
        MLP_IN = NODE_F + 3 * EDGE_F + GLOB_F
        col = edge_index[1]
        n = x.shape[0]
        out1 = jax.ops.segment_sum(edge_attr, col, num_segments=n)
        cnt = jax.ops.segment_sum(jnp.ones((edge_attr.shape[0], 1), edge_attr.dtype), col, num_segments=n)
        out2 = jax.ops.segment_max(edge_attr, col, num_segments=n)
        out2 = jnp.where(cnt > 0, out2, jnp.zeros_like(out2))
        out3 = out1 / jnp.maximum(cnt, 1.0)
        h = jnp.concatenate([x, out1, out2, out3, u[batch]], axis=1)
        h = jax.nn.relu(h @ W1 + b1) @ W2 + b2
        return h + x

    def _L0_ffn_ref(x, gate_w, gate_b, w1, b1, w2, b2, gamma, beta):
        import jax, jax.numpy as jnp
        import numpy as np
        B, S, H, F, E, K = (8, 512, 256, 512, 16, 2)
        EPS = 1e-05
        gate_logits = x @ gate_w + gate_b
        topk_vals, topk_idx = jax.lax.top_k(gate_logits, K)
        topk_w = jax.nn.softmax(topk_vals, axis=-1)
        h = jax.nn.relu(jnp.einsum('bsh,ehf->bsef', x, w1) + b1)
        expert_out = jnp.einsum('bsef,efh->bseh', h, w2) + b2
        sel = jnp.take_along_axis(expert_out, topk_idx[:, :, :, None], axis=2)
        moe = jnp.sum(topk_w[..., None] * sel, axis=2)
        y = x + moe
        mu = jnp.mean(y, axis=-1, keepdims=True)
        var = jnp.var(y, axis=-1, keepdims=True)
        return (y - mu) / jnp.sqrt(var + EPS) * gamma + beta
    edge_index = jnp.stack([src, dst])
    batch0 = jnp.zeros((6250,), jnp.int32)
    x = x + _L0_gnn_ref(_layernorm(x, axis=-1), edge_attr_96, L0_gnn_u, L0_gnn_W1, L0_gnn_b1, L0_gnn_W2, L0_gnn_b2, edge_index, batch0)
    x = x + _L0_ffn_ref(_layernorm(x, axis=-1)[None], L0_ffn_gate_w, L0_ffn_gate_b, L0_ffn_w1, L0_ffn_b1, L0_ffn_w2, L0_ffn_b2, L0_ffn_gamma, L0_ffn_beta)[0]
    return x

_drawn_inputs = setup_inputs


def setup_inputs(seed=0):
    import zlib

    import numpy as np

    out = dict(_drawn_inputs(seed))
    spreads = {'L0_ffn_gate_b': (0.0, 0.384),
     'L0_ffn_b1': (0.0, 0.8),
     'L0_ffn_b2': (0.0, 0.367),
     'L0_ffn_gamma': (1.0, 0.2),
     'L0_ffn_beta': (0.0, 0.274)}
    factors = {'L0_gnn_b1': 8.0, 'L0_gnn_b2': 8.0, 'L0_ffn_w1': 3.094}
    for name, (base, spread) in spreads.items():
        noise = np.random.default_rng([zlib.crc32(name.encode()), seed]).standard_normal(out[name].shape)
        drawn = base * np.exp(spread * noise) if base else spread * noise
        out[name] = jnp.asarray(drawn.astype(out[name].dtype))
    for name, factor in factors.items():
        out[name] = (out[name] * factor).astype(out[name].dtype)
    return out
```

```python
from contextlib import ExitStack

import concourse.bass as bass
from concourse import mybir

ALU = mybir.AluOpType
ACT = mybir.ActivationFunctionType
AX_X = mybir.AxisListType.X
F32 = mybir.dt.float32
I32 = mybir.dt.int32
U32 = mybir.dt.uint32

P = 128
FMAX = 3.4028234663852886e38
EPS = 1e-5
ROUND = 12582912.0


class Area:

    def __init__(self, mem, lo, hi):
        self.mem, self.at, self.hi = mem, lo, hi

    def take(self, *shape, parts=P, dt=F32):
        n = 1
        for s in shape:
            n *= s
        assert self.at + n <= self.hi, (self.at, n, self.hi)
        ap = self.mem[0:parts, self.at:self.at + n]
        self.at += n + n % 2
        if dt is not F32:
            ap = ap.bitcast(dt)
        if len(shape) > 1:
            names = [f"d{i}" for i in range(len(shape))]
            sizes = {k: v for k, v in zip(names[1:], shape[1:])}
            ap = ap.rearrange(f"p ({' '.join(names)}) -> p {' '.join(names)}", **sizes)
        return ap


class Steps:

    def __init__(self, eng, sem, base=0):
        self.eng, self.sem, self.base, self.n = eng, sem, base, 0

    def mark(self, ins):
        ins.then_inc(self.sem, 1)
        self.n += 1
        return self.n

    def wait(self, n=None):
        self.eng.wait_ge(self.sem, self.base + (self.n if n is None else n))


def in_pairs(eng, n, body, ahead=0, first=0):
    pairs = (n - ahead) // 2
    with eng.Fori(first // 2, pairs) as g:
        body(g * 2, g, 0)
        body(g * 2 + 1, g, 1)
    for i in range(2 * pairs, n):
        body(i, i // 2, i % 2)


def after(i, g, b, n=1):
    return i + n, g + (b + n) // 2, (b + n) % 2


def gnn_moe_kernel(nc, x, dst, edge_attr, u, gW1, gb1, gW2, gb2, gate_w, gate_b,
                   ew1, eb1, ew2, eb2, gamma, beta, out):
    N, D = x.shape
    E, EF = edge_attr.shape
    GF = u.shape[1]
    HID = gW1.shape[1]
    NX, _, FF = ew1.shape
    NT = 125
    TILES = N // NT
    MACROS = TILES // 2
    M = 2 * NT
    DC, HC, FC = D // P, HID // P, FF // P
    T = 80
    PIECES = E // T
    CHUNKS = -(-PIECES // P)
    FULL = CHUNKS - 1
    LASTP = PIECES - FULL * P
    LEVEL = 1
    LEVELS = CHUNKS // LEVEL
    ROWS = 500
    ROWE = E // ROWS
    SB = TILES // 2
    XB = 10
    SLOT_TILES = (2 * N - NX) // P + NX
    EW = DC * FF + FC * D
    CB = 5
    LAG = 14
    OB = 5
    EJ = NX * TILES
    HID_U = D + 3 * EF
    LINKS = [(lo, min(lo + 512, CHUNKS * P)) for lo in range(0, CHUNKS * P, 512)]
    assert TILES * NT == N and PIECES * T == E and ROWS * ROWE == E and TILES % SB == 0

    s_sum = nc.dram_tensor("run_sum", [E, EF], F32).ap()
    s_max = nc.dram_tensor("run_max", [E, EF], F32).ap()
    carry = nc.dram_tensor("piece_carry", [PIECES, 2 * EF], F32).ap()
    gnn_d = nc.dram_tensor("gnn_out", [N, D], F32).ap()
    x2_d = nc.dram_tensor("x2_normed", [N, D], F32).ap()
    x1b_d = nc.dram_tensor("x1_plus_beta", [N, D], F32).ap()
    ys_d = nc.dram_tensor("expert_rows", [SLOT_TILES * P, D], F32).ap()

    def by_macro(t):
        return t.rearrange("(i a p) d -> i p a d", a=2, p=NT)

    def by_tile(t):
        return t.rearrange("(i p) d -> i p d", p=NT)

    dst2 = dst.rearrange("(r c) -> r c", c=ROWE)
    dst_rows = dst.rearrange("(q t) -> q t", t=T)
    edges_q = edge_attr.rearrange("(q t) f -> q t f", t=T)
    sum_q = s_sum.rearrange("(q t) f -> q t f", t=T)
    max_q = s_max.rearrange("(q t) f -> q t f", t=T)

    with ExitStack() as ctx:
        def sem(name):
            return ctx.enter_context(nc.semaphore(name))

        TOTAL = 53200
        KEPT = 5160
        mem = ctx.enter_context(nc.sbuf_tensor("mem", [P, TOTAL], F32))
        A1 = KEPT + 3 * T * EF
        ROUTE_END = 18400
        k = Area(mem, 0, KEPT)
        ident = k.take(P)
        upper = k.take(NT, parts=NT)
        shift = k.take(NT, parts=NT)
        corner = k.take(NT, parts=NT)
        ones = k.take(ROWS)
        zeros = k.take(P)
        numbers = k.take(P)
        b1col = k.take(HC)
        cbias = k.take(HC)
        b2bc = k.take(2, D, parts=NT)
        gammabc = k.take(D, parts=NT)
        betabc = k.take(2, D, parts=NT)
        gwt = k.take(DC, NX)
        gbbc = k.take(NX, parts=NT)
        eb1c = k.take(NX, FC)
        epsc = k.take(1)
        node = k.take(TILES, parts=NT)
        firsts, inrow, endn, startn, has, cp, cb, rch, tA, tB = (k.take(TILES, parts=NT) for _ in range(10))
        wsel = k.take(2, TILES, parts=NT)
        IX = k.take(TILES, 2, parts=NT, dt=U32)
        rowU = k.take(TILES, parts=NT, dt=U32)
        rstd, nmr, rpow = (k.take(TILES, parts=NT) for _ in range(3))
        stat = [k.take(6, parts=NT) for _ in range(4)]
        sum_now = [k.take(XB, parts=NT) for _ in range(2)]
        nmean, dev2 = (k.take(TILES, parts=NT) for _ in range(2))
        Lo = k.take(TILES, NX, parts=NT)
        gatef = k.take(MACROS, parts=1)
        gatei = k.take(MACROS, parts=1, dt=I32)
        posU = k.take(2, TILES, parts=NT, dt=U32)
        slotU = k.take(SLOT_TILES, dt=U32)
        slot_now = [k.take(1, dt=U32) for _ in range(2)]
        pos_now = [k.take(2, CB, parts=NT, dt=U32) for _ in range(2)]
        texp = k.take(SLOT_TILES, parts=1, dt=I32)
        mvt2 = [k.take(2, 2, parts=NT) for _ in range(2)]
        sd_now = [k.take(2, parts=NT) for _ in range(2)]
        rs_now = [k.take(2, parts=NT) for _ in range(2)]
        mvc = [k.take(CB, 2, parts=NT) for _ in range(2)]
        statc = [k.take(CB, 6, parts=NT) for _ in range(2)]
        sdc = [k.take(CB, parts=NT) for _ in range(2)]
        rsc = [k.take(CB, parts=NT) for _ in range(2)]
        nmc = [k.take(CB, parts=NT) for _ in range(2)]

        a = Area(mem, KEPT, A1)
        Eb = [a.take(T, EF) for _ in range(2)]
        Sb = a.take(T, EF)
        wexp = mem[:, ROUTE_END:ROUTE_END + NX * EW].rearrange("p (e w) -> p e w", e=NX)
        wexp1 = wexp[:, :, 0:DC * FF].rearrange("p e (c f) -> p e c f", c=DC)
        wexp2 = wexp[:, :, DC * FF:EW].rearrange("p e (c d) -> p e c d", c=FC)
        LN2 = A1 - 2 * (3 * 2 * D + 2 * D)
        a = Area(mem, LN2, A1)
        Lx = [a.take(2, D, parts=NT) for _ in range(2)]
        Ln = [a.take(2, D, parts=NT) for _ in range(2)]
        Lg = [a.take(2, D, parts=NT) for _ in range(2)]
        Lb = [a.take(2, D, parts=NT) for _ in range(2)]
        X2T_AT = ROUTE_END - 2 * (DC * M + 2 * D)
        EARLY = (LN2 - ROUTE_END) // EW

        a = Area(mem, A1, TOTAL)
        W_AT = a.at
        W1x = a.take(DC, HID)
        W1a = a.take(3, HID, parts=EF)
        W2 = a.take(HC, D)
        W1u = a.take(HID, parts=GF)
        u0 = a.take(1, parts=GF)
        WORK = a.at
        XR = [a.take(2, D, parts=NT) for _ in range(2)]
        XN = [a.take(2, D, parts=NT) for _ in range(2)]
        GM = [a.take(2, EF, parts=NT) for _ in range(2)]
        GS = [a.take(2, EF, parts=NT) for _ in range(2)]
        GC = [a.take(2, 2 * EF, parts=NT) for _ in range(2)]
        IXn = [a.take(2, 2, parts=NT, dt=U32) for _ in range(2)]
        CS = [a.take(2, EF, parts=NT) for _ in range(2)]
        diff, take_c, take_p = (a.take(2, EF, parts=NT) for _ in range(3))
        RAW = [a.take(2, 2, EF, parts=NT) for _ in range(2)]
        NB = [a.take(2, 3, EF, parts=NT) for _ in range(2)]
        XT = [a.take(DC, M) for _ in range(2)]
        AT = [a.take(3, M, parts=EF) for _ in range(2)]
        H = a.take(HC, M)
        GO = a.take(2, D, parts=NT)
        WORK_END = a.at
        Dst = a.take(CHUNKS, T, dt=I32)
        Kk = a.take(CHUNKS, T)
        Kx = Dst.bitcast(F32)
        L = a.take(CHUNKS * P, parts=64)
        CT = [a.take(3, P, parts=64) for _ in range(2)]
        CR = [a.take(2, EF) for _ in range(2)]
        a = Area(mem, WORK, WORK_END)
        rowI = a.take(ROWS, parts=1, dt=I32)
        rowF = a.take(ROWS, parts=1)
        tailI = a.take(PIECES, parts=1, dt=I32)
        tailF = a.take(PIECES, parts=1)
        Lrow = a.take(CHUNKS * P, parts=1)
        SR = a.take(SB, ROWE, parts=NT, dt=I32)
        junk = a.take(ROWS, parts=NT)
        a = Area(mem, W_AT, WORK)
        XA = [a.take(XB, D, parts=NT) for _ in range(2)]
        dropped = [a.take(D, parts=NT) for _ in range(2)]
        a = Area(mem, X2T_AT, ROUTE_END)
        x2T = [a.take(DC, M) for _ in range(2)]
        X2now = [a.take(2, D, parts=NT) for _ in range(2)]
        a = Area(mem, KEPT, X2T_AT)
        Oa, Ob, Rk, ioe = (a.take(TILES, NX, parts=NT) for _ in range(4))
        both, tot, incl, keepm = (a.take(NX, TILES, parts=NT) for _ in range(4))
        eO, eT, eN, eI, eE = (a.take(NX, parts=NT) for _ in range(5))
        hiq = a.take(2, TILES, parts=NT)
        loq = a.take(2, TILES, parts=NT)


        v0 = a.take(2, TILES, parts=NT)
        one_hot = a.at
        OL = [a.take(OB, P, parts=NT) for _ in range(2)]
        OH = [a.take(OB, SLOT_TILES, parts=NT) for _ in range(2)]
        a = Area(mem, one_hot, X2T_AT)
        tcmp = a.take(SLOT_TILES, NX, parts=1)
        tsum = a.take(SLOT_TILES, parts=1)
        a = Area(mem, KEPT, ROUTE_END)
        XG = [a.take(D) for _ in range(2)]
        XgT = [a.take(DC, P) for _ in range(2)]
        hraw = [a.take(FF) for _ in range(2)]
        hT = [a.take(FC, P) for _ in range(2)]
        YO = [a.take(D) for _ in range(2)]
        eb2bc = a.take(NX, D)
        a = Area(mem, ROUTE_END, TOTAL)
        ER = [a.take(2, CB, D, parts=NT) for _ in range(2)]
        EX = [a.take(CB, D, parts=NT) for _ in range(2)]
        EB = [a.take(CB, D, parts=NT) for _ in range(2)]
        Y1 = [a.take(CB, D, parts=NT) for _ in range(2)]
        Y2 = [a.take(CB, D, parts=NT) for _ in range(2)]
        Y3 = [a.take(CB, D, parts=NT) for _ in range(2)]
        Y4 = [a.take(CB, D, parts=NT) for _ in range(2)]

        ps = ctx.enter_context(nc.psum_tensor("ps", [P, 8 * 512], F32))

        def bank(n, lo=0, hi=512, parts=P):
            return ps[0:parts, n * 512 + lo:n * 512 + hi]

        ld_dst, ld_par, consts, consts_step = sem("ld_dst"), sem("ld_par"), sem("consts_ready"), sem("consts_step")
        dve_setup, dve_search, dve_counts = sem("dve_setup"), sem("firsts_counted"), sem("rows_counted")
        bc_firsts, bc_tails, heads_f, tails_f = sem("firsts_spread"), sem("tails_spread"), sem("firsts_float"), sem("tails_float")
        rows_ready, row_read = sem("rows_ready"), sem("row_read")
        row_got = sem("rows_got")
        ends_ready, starts_psum, index_ready = sem("ends_ready"), sem("starts_psum"), sem("index_ready")
        cbias_psum, cbias_ready = sem("cbias_psum"), sem("cbias_ready")
        stats_step, var_ready, norm1_step, rstd_ready = sem("moments_step"), sem("deviations_ready"), sem("norm1_step"), sem("rstd_ready")
        xa_got = [sem(f"xa_got{i}") for i in range(2)]
        setup_done = sem("setup_done")
        e_got = [sem(f"edges_got{i}") for i in range(2)]
        sum_scanned, max_scanned, carry_step, carry_ready = sem("sum_scanned"), sem("max_scanned"), sem("carry_step"), sem("carry_ready")
        st_sum = sem("sum_stored")
        st_max = [sem(f"max_stored{i}") for i in range(2)]
        st_car = [sem(f"carry_stored{i}") for i in range(2)]
        chunk_done = sem("chunk_in_dram")
        gathered = [sem(f"gathered{i}") for i in range(2)]
        diffed, picked = sem("diffed"), sem("picked")
        pick_step = sem("pick_step")
        ix_copied, carried, joined, node_rows = sem("ix_copied"), sem("carried"), sem("joined"), sem("node_rows")
        turned, turned_out = sem("turned"), sem("turned_out")
        h_psum, h_ready, g_psum, g_out = sem("h_psum"), sem("h_ready"), sem("g_psum"), sem("g_out")
        go_stored = sem("gnn_rows_stored")
        ln_got = [sem(f"norm2_rows_got{i}") for i in range(2)]
        ln_read, ln_step, x1b_ready = sem("norm2_rows_read"), sem("norm2_step"), sem("x1b_ready")
        x1b_stored = [sem(f"x1b_stored{i}") for i in range(2)]
        x2_st = [sem(f"x2_rows_stored{i}") for i in range(2)]
        x2_rows, x2_stored, x2_turned, x2_out, logits, logits_out, eb2_loaded = sem("x2_rows"), sem("x2_stored"), sem("x2_turned"), sem("x2_turned_out"), sem("logits"), sem("logits_out"), sem("eb2_loaded")
        route, prefix_in, prefix_out, gap_ready, e_gap, slots_in = sem("route_step"), sem("prefix_in"), sem("prefix_out"), sem("gap_ready"), sem("e_gap"), sem("hi_lo_ready")
        ol_ready, oh_ready, hot_used = sem("lo_hot_ready"), sem("hi_hot_ready"), sem("one_hots_used")
        slots_psum, slots_ready, pos_ready, texp_ready, w_loaded = sem("slots_psum"), sem("slots_ready"), sem("pos_ready"), sem("tile_experts_ready"), sem("expert_weights_loaded")
        slot_copied = sem("slot_copied")
        xg_got = [sem(f"slot_rows_got{i}") for i in range(2)]
        xt_psum, xt_ready, h1_psum, h1_ready = sem("xt_psum"), sem("xt_ready"), sem("h1_psum"), sem("h1_ready")
        h2_psum, h2_ready, y_psum, y_ready = sem("h2_psum"), sem("h2_ready"), sem("y_psum"), sem("y_ready")
        yo_stored = [sem(f"expert_rows_stored{i}") for i in range(2)]
        ys_all = sem("expert_rows_all")
        pos_copied, er_read = sem("pos_copied"), sem("combine_rows_read")
        er_got = [sem(f"combine_rows_got{i}") for i in range(2)]
        ex_got = [sem(f"combine_x2_got{i}") for i in range(2)]
        eb_got = [sem(f"combine_x1b_got{i}") for i in range(2)]
        var2_ready, sd2_ready, rs2_ready = sem("norm2_var_ready"), sem("norm2_sd_ready"), sem("norm2_rstd_ready")
        c_step, c_var, c_sd, c_nm, c_norm, c_last, c_out = (sem(f"combine_{n}") for n in ("step", "var", "sd", "shift", "norm", "last", "out"))
        out_stored = [sem(f"out_stored{i}") for i in range(2)]
        dve_free = sem("dve_done_with_route")
        passed = sem("waits_passed")

        def hold(eng, sem, value):
            eng.wait_ge(sem, value)
            eng.sem_inc(passed, 1)

        def row(ap, parts):
            return ap.rearrange("(o n) -> o n", o=1).to_broadcast([parts, ap.shape[0]])

        def spread(ap, axis, n):
            shape = list(ap.shape)
            shape.insert(axis, n)
            return ap.unsqueeze(axis).to_broadcast(shape)

        block = ctx.enter_context(nc.Block())

        @block.sync
        def _(sp):
            sp.dma_start(Dst[:, 0:FULL, :], dst_rows[0:FULL * P, :].rearrange("(s p) t -> p s t", p=P)).then_inc(ld_dst, 16)
            sp.dma_start(Dst[0:LASTP, FULL, :], dst_rows[FULL * P:PIECES, :]).then_inc(ld_dst, 16)
            sp.dma_start(Eb[0][:], edges_q[0:P]).then_inc(e_got[0], 16)
            sp.dma_start(rowI, dst2[:, 0:1].rearrange("r o -> o r"), allow_slow_non_contiguous=True).then_inc(ld_dst, 16)
            sp.dma_start(tailI, dst_rows[:, T - 1:T].rearrange("r o -> o r"), allow_slow_non_contiguous=True).then_inc(ld_dst, 16)


            sp.dma_start(Eb[1][:], edges_q[P:2 * P]).then_inc(e_got[1], 16)

            def edge_chunk(s, g, b):
                parts = LASTP if isinstance(s, int) and s == FULL else P
                sp.wait_ge(sum_scanned, s + 1)
                sp.dma_start(sum_q[bass.ds(s * P, parts)], Sb[0:parts]).then_inc(st_sum, 16)
                sp.wait_ge(max_scanned, s + 1)
                sp.dma_start(max_q[bass.ds(s * P, parts)], Eb[b][0:parts]).then_inc(st_max[b], 16)
                sp.wait_ge(carry_ready, s + 1)
                sp.dma_start(carry[bass.ds(s * P, parts)], CR[b][0:parts].rearrange("p s f -> p (s f)")).then_inc(st_car[b], 16)
                sp.wait_ge(st_sum, (s + 2) * 16)
                sp.wait_ge(st_max[b], (g + 1) * 16)
                sp.wait_ge(st_car[b], (g + 1) * 16)
                sp.sem_inc(chunk_done, 1)
                if not isinstance(s, int) or s + 2 < CHUNKS:
                    more = LASTP if isinstance(s, int) and s + 2 == FULL else P
                    sp.dma_start(Eb[b][0:more], edges_q[bass.ds((s + 2) * P, more)]).then_inc(e_got[b], 16)
            in_pairs(sp, CHUNKS, edge_chunk, ahead=4)

            def expert_weights(e):
                sp.dma_start(wexp1[:, bass.ds(e, 1)], ew1[bass.ds(e, 1)].rearrange("e (c p) f -> p e c f", p=P)).then_inc(w_loaded, 16)
                sp.dma_start(wexp2[:, bass.ds(e, 1)], ew2[bass.ds(e, 1)].rearrange("e (c p) d -> p e c d", p=P)).then_inc(w_loaded, 16)
            for e in range(EARLY):
                expert_weights(e)

            def norm2_rows(i, g, b):
                sp.wait_ge(ln_read, i + 1)
                sp.dma_start(Lx[b], by_macro(x)[bass.ds(i, 1)]).then_inc(ln_got[b], 16)
                sp.wait_ge(go_stored, (i + 2) * 16)
                sp.dma_start(Lg[b], by_macro(gnn_d)[bass.ds(i, 1)]).then_inc(ln_got[b], 16)

            def norm2_load_and_store(i, g, b):
                sp.wait_ge(x1b_ready, i + 1)
                sp.dma_start(by_macro(x1b_d)[bass.ds(i, 1)], Lb[b]).then_inc(x1b_stored[b], 16)
                sp.wait_ge(x2_rows, i + 1)
                sp.dma_start(by_macro(x2_d)[bass.ds(i, 1)], X2now[b]).then_inc(x2_st[b], 16)
                if not isinstance(i, int) or i + 2 < MACROS:
                    norm2_rows(*after(i, g, b, 2))
            norm2_rows(0, 0, 0)
            norm2_rows(1, 0, 1)
            in_pairs(sp, MACROS, norm2_load_and_store, ahead=2)
            sp.wait_ge(x1b_stored[0], (MACROS - MACROS // 2 + 1) * 16)
            sp.wait_ge(x1b_stored[1], (MACROS // 2 + 1) * 16)
            sp.wait_ge(x2_st[0], (MACROS - MACROS // 2 + 1) * 16)
            sp.wait_ge(x2_st[1], (MACROS // 2 + 1) * 16)
            sp.sem_inc(x2_stored, 1)
            with sp.Fori(EARLY, NX) as e:
                expert_weights(e)
            sp.wait_ge(dve_free, 1)
            sp.dma_start(eb2bc, eb2.rearrange("(o e) d -> o e d", o=1).to_broadcast([P, NX, D])).then_inc(eb2_loaded, 16)


            def store_y(i, g, b):
                sp.wait_ge(y_ready, i + 3)
                sp.dma_start(ys_d[bass.ds(i * P, P)], YO[b]).then_inc(yo_stored[b], 16)
            in_pairs(sp, SLOT_TILES, store_y)
            sp.wait_ge(yo_stored[0], (SLOT_TILES - SLOT_TILES // 2 + 1) * 16)
            sp.wait_ge(yo_stored[1], (SLOT_TILES // 2 + 1) * 16)
            sp.sem_inc(ys_all, 1)

            by_batch = "(i a p) d -> i p a d"

            def load_x2(i, b):
                sp.dma_start(EX[b], x2_d.rearrange(by_batch, a=CB, p=NT)[bass.ds(i, 1)]).then_inc(ex_got[b], 16)

            def load_x1b(i, b):
                sp.dma_start(EB[b], x1b_d.rearrange(by_batch, a=CB, p=NT)[bass.ds(i, 1)]).then_inc(eb_got[b], 16)
            for b in range(2):
                load_x2(b, b)
                load_x1b(b, b)

            def store_out(i, g, b):
                more = not isinstance(i, int) or i + 2 < TILES // CB
                if more:
                    sp.wait_ge(er_read, i + 3)
                    load_x2(i + 2, b)
                sp.wait_ge(c_out, i + 1)
                if more:
                    load_x1b(i + 2, b)
                sp.dma_start(out.rearrange(by_batch, a=CB, p=NT)[bass.ds(i, 1)], Y4[b]).then_inc(out_stored[b], 16)
            in_pairs(sp, TILES // CB, store_out, ahead=2)
            sp.wait_ge(out_stored[0], (TILES // CB // 2 + 1) * 16)
            sp.wait_ge(out_stored[1], (TILES // CB // 2 + 1) * 16)

        @block.gpsimd
        def _(pool):
            st = Steps(pool, consts_step)
            st.mark(pool.memset(ident, 0.0))
            st.mark(pool.memset(upper, 1.0))
            st.mark(pool.memset(shift, 0.0))
            st.mark(pool.memset(corner, 0.0))
            st.mark(pool.memset(ones, 1.0))
            st.mark(pool.memset(zeros, 0.0))
            st.mark(pool.memset(epsc, EPS))
            st.mark(pool.iota(numbers, pattern=[[1, P]], base=0, channel_multiplier=0,
                              allow_small_or_imprecise_dtypes=True))
            st.mark(pool.iota(node, pattern=[[NT, TILES]], base=0, channel_multiplier=1,
                              allow_small_or_imprecise_dtypes=True))
            st.wait()
            pool.affine_select(out=ident, in_=ident, compare_op=ALU.not_equal, fill=1.0, base=0,
                               pattern=[[-1, P]], channel_multiplier=1)
            pool.affine_select(out=upper, in_=upper, compare_op=ALU.is_gt, fill=0.0, base=0,
                               pattern=[[1, NT]], channel_multiplier=-1)
            pool.affine_select(out=shift, in_=shift, compare_op=ALU.not_equal, fill=1.0, base=1,
                               pattern=[[-1, NT]], channel_multiplier=1)
            pool.affine_select(out=corner, in_=corner, compare_op=ALU.not_equal, fill=1.0, base=-(NT - 1),
                               pattern=[[-1000, NT]], channel_multiplier=1).then_inc(consts, 1)

            s1 = Steps(pool, norm1_step)
            pool.wait_ge(var_ready, 1)
            s1.mark(pool.memset(rpow, -0.5))
            s1.mark(pool.tensor_scalar(rstd, dev2, 1.0 / D, EPS, ALU.mult, ALU.add))
            s1.wait()
            s1.mark(pool.tensor_tensor(rstd, rstd, rpow, ALU.pow))
            s1.wait()
            pool.tensor_tensor(nmr, nmean, rstd, ALU.mult).then_inc(rstd_ready, 1)

            pool.wait_ge(rows_ready, 1)
            for half in range(2):
                if half:
                    pool.wait_ge(row_read, SB + 1)
                for m in range(SB):
                    pool.indirect_dma_start(out=SR[:, m, :], out_offset=None, in_=dst2,
                                            in_offset=bass.IndirectOffsetOnAxis(rowU[:, half * SB + m:half * SB + m + 1], 0)).then_inc(row_got, 16)

            pool.wait_ge(index_ready, 1)
            pool.wait_ge(setup_done, 1)

            def gather(i, g, b):
                level = pool.value_load(gatei[0:1, bass.ds(i, 1)], min_val=1, max_val=LEVELS)
                hold(pool, turned, i + 1)
                pool.tensor_copy(IXn[b], IX[:, bass.ds(2 * i, 2), :]).then_inc(ix_copied, 1)
                pool.wait_ge(ix_copied, i + 1)
                hold(pool, chunk_done, level * LEVEL)
                for lv in range(1, LEVELS + 1):
                    edges, pieces = min(E, lv * LEVEL * P * T), min(PIECES, lv * LEVEL * P)
                    with pool.If(level == lv):
                        for a in range(2):
                            last, before = (bass.IndirectOffsetOnAxis(IXn[b][:, a, n:n + 1], 0) for n in range(2))
                            pool.indirect_dma_start(out=GM[b][:, a, :], out_offset=None, in_=s_max[0:edges], in_offset=last).then_inc(gathered[b], 16)
                            pool.indirect_dma_start(out=GS[b][:, a, :], out_offset=None, in_=s_sum[0:edges], in_offset=last).then_inc(gathered[b], 16)
                            pool.indirect_dma_start(out=GC[b][:, a, :], out_offset=None, in_=carry[0:pieces], in_offset=before).then_inc(gathered[b], 16)
                pool.dma_start(XR[b], by_macro(x)[bass.ds(i, 1)]).then_inc(gathered[b], 16)

            def join(i, g, b):
                before = GC[b][:, :, EF:2 * EF]
                pool.wait_ge(gathered[b], (g + 1) * 7 * 16)
                pool.wait_ge(joined, i + 1)
                pool.tensor_tensor(diff, before, GM[b], ALU.subtract).then_inc(diffed, 1)
                pool.wait_ge(carried, i + 1)
                pool.tensor_tensor(RAW[b][:, :, 0, :], GS[b], CS[b], ALU.add)
                pool.tensor_tensor(take_c, before, take_c, ALU.mult)
                pool.tensor_tensor(take_p, GM[b], take_p, ALU.mult).then_inc(picked, 1)
                pool.wait_ge(picked, i + 1)
                pool.tensor_tensor(RAW[b][:, :, 1, :], take_c, take_p, ALU.add).then_inc(joined, 1)

            def gather_and_join(i, g, b):
                gather(i, g, b)
                join(i, g, b)
            pool.sem_inc(joined, 1)
            in_pairs(pool, MACROS, gather_and_join)

            pool.wait_ge(x2_stored, 1)
            pool.wait_ge(slots_ready, 1)
            pool.wait_ge(dve_free, 1)

            def slot_rows(i, g, b):
                hold(pool, xt_psum, i + 1)
                pool.tensor_copy(slot_now[b], slotU[:, bass.ds(i, 1)]).then_inc(slot_copied, 1)
                hold(pool, slot_copied, i + 1)
                pool.indirect_dma_start(out=XG[b], out_offset=None, in_=x2_d,
                                        in_offset=bass.IndirectOffsetOnAxis(slot_now[b], 0)).then_inc(xg_got[b], 16)
            in_pairs(pool, SLOT_TILES, slot_rows)

            pool.wait_ge(ys_all, 1)

            def expert_rows(i, g, b):
                hold(pool, er_read, i + 1)
                pool.tensor_copy(pos_now[b], posU[:, :, bass.ds(i * CB, CB)]).then_inc(pos_copied, 1)
                hold(pool, pos_copied, i + 1)
                for m in range(CB):
                    for kk in range(2):
                        pool.indirect_dma_start(out=ER[b][:, kk, m, :], out_offset=None, in_=ys_d,
                                                in_offset=bass.IndirectOffsetOnAxis(pos_now[b][:, kk, m:m + 1], 0)).then_inc(er_got[b], 16)
            in_pairs(pool, TILES // CB, expert_rows)

        @block.scalar
        def _(act):
            def param(dst_ap, src, slow=False):
                act.dma_start(dst_ap, src, allow_slow_non_contiguous=slow).then_inc(ld_par, 16)
            for b in range(2):
                act.dma_start(XA[b], x.rearrange("(i a p) d -> i p a d", a=XB, p=NT)[b:b + 1]).then_inc(xa_got[b], 16)
            param(W1u, gW1[HID_U:HID_U + GF, :])
            param(u0, u[0:1, :].rearrange("o g -> g o"), slow=True)
            param(b1col, gb1.rearrange("(c p) -> p c", p=P), slow=True)
            param(b2bc, spread(row(gb2, NT), 1, 2))
            param(betabc, spread(row(beta, NT), 1, 2))
            param(gammabc, row(gamma, NT))
            param(gwt, gate_w.rearrange("(c p) e -> p c e", p=P))
            param(gbbc, row(gate_b, NT))
            param(eb1c, eb1.rearrange("e (c p) -> p e c", p=P), slow=True)
            act.sem_inc(go_stored, 16)

            def moments(i, b, more):
                s1 = Steps(act, stats_step, i * (2 * XB + 1))
                act.wait_ge(xa_got[b], (i // 2 + 1) * 16)
                for a in range(XB):
                    s1.mark(act.activation(dropped[a % 2], XA[b][:, a, :], ACT.Identity, scale=-1.0 / D, accum_out=sum_now[b][:, a:a + 1]))
                    act.wait_ge(stats_step, s1.base + s1.n - (a < XB - 1))
                for a in range(XB):
                    s1.mark(act.activation(dropped[a % 2], XA[b][:, a, :], ACT.Square, bias=sum_now[b][:, a:a + 1], accum_out=dev2[:, XB * i + a:XB * i + a + 1]))
                    act.wait_ge(stats_step, s1.base + s1.n - (a < XB - 1))
                s1.mark(act.activation(nmean[:, XB * i:XB * i + XB], sum_now[b], ACT.Identity))
                s1.wait()
                if more:
                    act.dma_start(XA[b], x.rearrange("(i a p) d -> i p a d", a=XB, p=NT)[i + 2:i + 3]).then_inc(xa_got[b], 16)
            for i in range(TILES // XB):
                moments(i, i % 2, i + 2 < TILES // XB)
            act.sem_inc(var_ready, 1)
            param(W1x, gW1[0:D, :].rearrange("(c p) h -> p c h", p=P))
            param(W1a, gW1[D:D + 3 * EF, :].rearrange("(s f) h -> f s h", f=EF))
            param(W2, gW2.rearrange("(c p) d -> p c d", p=P))

            def carry_in(i, g, b):
                act.wait_ge(gathered[b], (g + 1) * 7 * 16)
                for a in range(2):
                    act.activation(CS[b][:, a, :], GC[b][:, a, 0:EF], ACT.Identity, scale=cp[:, bass.ds(2 * i + a, 1)])
                hold(act, diffed, i + 1)
                for a in range(2):
                    act.activation(take_p[:, a, :], diff[:, a, :], ACT.Sign, scale=cp[:, bass.ds(2 * i + a, 1)]).then_inc(pick_step, 1)
                act.wait_ge(pick_step, 3 * i + 2)
                act.activation(take_c, take_p, ACT.Relu).then_inc(pick_step, 1)
                act.wait_ge(pick_step, 3 * i + 3)
                act.activation(take_p, take_c, ACT.Identity, bias=ones[0:NT, 0:1], scale=-1.0).then_inc(carried, 1)

            def mask_rows(i, g, b):
                act.wait_ge(joined, i + 2)
                for a in range(2):
                    j = bass.ds(2 * i + a, 1)
                    act.activation(NB[b][:, a, 0:2, :], RAW[b][:, a, :, :], ACT.Identity, scale=has[:, j])
                    act.activation(XN[b][:, a, :], XR[b][:, a, :], ACT.Identity, bias=nmr[:, j], scale=rstd[:, j])
                    ins = act.activation(NB[b][:, a, 2, :], RAW[b][:, a, 0, :], ACT.Identity, scale=rch[:, j])
                ins.then_inc(node_rows, 1)

            def take_turned(i, g, b):
                act.wait_ge(turned, i + 3)
                act.activation(XT[b], bank(0, 0, DC * M).rearrange("p (c n) -> p c n", c=DC), ACT.Identity)
                act.activation(AT[b][:, 0:2, :], bank(1, 0, 2 * M, EF).rearrange("p (s n) -> p s n", s=2), ACT.Identity)
                act.activation(AT[b][:, 2, :], bank(2, 0, M, EF), ACT.Identity).then_inc(turned_out, 1)

            def relu(i, g, hc):
                act.wait_ge(h_psum, i * HC + hc + 1)
                if hc == 0:
                    act.wait_ge(g_psum, 2 * i + 2)
                act.activation(H[:, hc, :], bank(3 + hc % 2, 0, M), ACT.Relu, bias=cbias[:, hc:hc + 1]).then_inc(h_ready, 1)

            def root(r, b):
                act.wait_ge(var2_ready, r + 1)
                act.activation(sd_now[b], mvt2[b][:, :, 1], ACT.Sqrt, bias=epsc[0:NT]).then_inc(sd2_ready, 1)

            def take_x2(r, b):
                act.wait_ge(x2_turned, r + 3)
                act.wait_ge(logits, r + 1)
                act.activation(x2T[b], bank(7, 0, DC * M).rearrange("p (c n) -> p c n", c=DC), ACT.Identity).then_inc(x2_out, 1)

            def take_logits(r, b):
                act.wait_ge(logits, r + 3)
                act.activation(Lo[:, bass.ds(2 * r, 2), :], bank(7, 0, 2 * NX, NT).rearrange("p (a e) -> p a e", a=2),
                               ACT.Identity).then_inc(logits_out, 1)

            def gnn_step(i, g, b, route_too=True):
                more = not isinstance(i, int) or i + 1 < MACROS
                r = 2 * (i - LAG)
                for hc in range(HC):
                    if more and hc == 1:
                        carry_in(*after(i, g, b))
                    if more and hc == 5:
                        mask_rows(*after(i, g, b))
                    if route_too and hc == 3:
                        take_x2(r, 0)
                    relu(i, g, hc)
                if route_too:
                    take_logits(r, 0)
                    root(r + 2, 0)
                if more:
                    take_turned(*after(i, g, b))
                act.wait_ge(go_stored, (i + 1) * 16)
                for a in range(2):
                    act.wait_ge(g_psum, 2 * i + a + 3)
                    ins = act.activation(GO[:, a, :], bank(5 + a, 0, D, NT), ACT.Identity)
                    if route_too and a == 0:
                        take_x2(r + 1, 1)
                ins.then_inc(g_out, 1)
                act.wait_ge(g_out, i + 2)
                act.dma_start(by_macro(gnn_d)[bass.ds(i, 1)], GO).then_inc(go_stored, 16)
                if route_too:
                    take_logits(r + 1, 1)
                    root(r + 3, 1)
            act.wait_ge(cbias_ready, 1)
            act.wait_ge(rstd_ready, 1)
            carry_in(0, 0, 0)
            mask_rows(0, 0, 0)
            take_turned(0, 0, 0)
            in_pairs(act, LAG, lambda i, g, b: gnn_step(i, g, b, route_too=False))
            root(0, 0)
            root(1, 1)
            in_pairs(act, MACROS, gnn_step, ahead=1, first=LAG)
            for r in range(2 * (MACROS - LAG), MACROS):
                take_x2(r, r % 2)
                take_logits(r, r % 2)
                if r + 2 < MACROS:
                    root(r + 2, r % 2)

            act.wait_ge(gap_ready, 1)
            act.activation(v0[:, 1, :], v0[:, 0, :], ACT.Exp).then_inc(e_gap, 1)

            act.wait_ge(texp_ready, 1)

            def expert_relu(i, g, b):
                e = act.value_load(texp[0:1, bass.ds(i, 1)], min_val=0, max_val=NX - 1)
                act.wait_ge(h2_psum, i + 1)
                act.wait_ge(y_psum, i + 1)
                for c in range(FC):
                    ins = act.activation(hT[b][:, c, :], bank(4 + b, c * P, (c + 1) * P), ACT.Relu,
                                         bias=eb1c[:, bass.ds(e, 1), c])
                ins.then_inc(h2_ready, 1)
            in_pairs(act, SLOT_TILES, expert_relu)

            def combine_norm(i, g, b):
                act.wait_ge(c_var, i + 1)
                act.activation(sdc[b], mvc[b][:, :, 1], ACT.Sqrt, bias=epsc[0:NT]).then_inc(c_sd, 1)
                act.wait_ge(c_nm, i + 1)
                act.wait_ge(c_last, i + 1)
                for m in range(CB):
                    ins = act.activation(Y3[b][:, m, :], Y2[b][:, m, :], ACT.Identity, bias=nmc[b][:, m:m + 1], scale=rsc[b][:, m:m + 1])
                ins.then_inc(c_norm, 1)
            in_pairs(act, TILES // CB, combine_norm)

        @block.tensor
        def _(pe):
            for sm, n in ((turned, 2), (turned_out, 1), (h_ready, 2), (g_psum, 2), (g_out, 1), (logits, 2), (x2_out, 1), (logits_out, 1),
                          (hot_used, 2), (x2_turned, 2), (xt_psum, 2), (xt_ready, 2), (h1_ready, 2), (h2_ready, 2), (y_psum, 2), (y_ready, 2)):
                pe.sem_inc(sm, n)

            pe.wait_ge(consts, 1)
            pe.wait_ge(heads_f, 1)
            pe.matmul(bank(0, 0, ROWS, NT), ones[0:1, 0:NT], rowF, start=True, stop=True).then_inc(bc_firsts, 1)
            pe.wait_ge(tails_f, 1)
            for n, (lo, hi) in enumerate(LINKS):
                ins = pe.matmul(bank(1 + n, 0, hi - lo, 64), ones[0:1, 0:64], Lrow[:, lo:hi], start=True, stop=True)
            ins.then_inc(bc_tails, 1)
            pe.wait_ge(ld_par, 12 * 16)
            for hc in range(HC):
                ins = pe.matmul(bank(4, hc, hc + 1), W1u[:, hc * P:(hc + 1) * P], u0, start=True, stop=True)
            ins.then_inc(cbias_psum, 1)
            pe.wait_ge(ends_ready, 1)
            pe.matmul(bank(5, 0, TILES, NT), shift, endn, start=True, stop=False)
            pe.matmul(bank(5, 1, TILES, NT), corner, endn[:, 0:TILES - 1], start=False, stop=True).then_inc(starts_psum, 1)
            pe.wait_ge(index_ready, 1)
            pe.wait_ge(cbias_ready, 1)

            def turn(i, g, b):
                pe.wait_ge(node_rows, i + 1)
                pe.wait_ge(turned_out, i + 1)
                for a in range(2):
                    for c in range(DC):
                        pe.transpose(bank(0, c * M + a * NT, c * M + (a + 1) * NT), XN[b][:, a, c * P:(c + 1) * P], ident[0:NT, 0:NT])
                    for s in range(3):
                        ins = pe.transpose(bank(1 + s // 2, s % 2 * M + a * NT, s % 2 * M + (a + 1) * NT, EF), NB[b][:, a, s, :], ident[0:NT, 0:NT])
                ins.then_inc(turned, 1)

            def layer1(i, g, b, between=None):
                pe.wait_ge(turned_out, i + 2)
                for hc in range(HC):
                    pe.wait_ge(h_ready, i * HC + hc + 1)
                    h = bank(3 + hc % 2, 0, M)
                    for c in range(DC):
                        pe.matmul(h, W1x[:, c, hc * P:(hc + 1) * P], XT[b][:, c, :], start=(c == 0), stop=False)
                    for s in range(3):
                        ins = pe.matmul(h, W1a[:, s, hc * P:(hc + 1) * P], AT[b][:, s, :], start=False, stop=(s == 2))
                    ins.then_inc(h_psum, 1)
                    if between and hc == 1:
                        between()

            def layer2(i, g, b, between=None):
                pe.wait_ge(h_ready, i * HC + HC + 2)
                pe.wait_ge(g_out, i + 1)
                for a in range(2):
                    for hc in range(HC):
                        ins = pe.matmul(bank(5 + a, 0, D, NT), H[:, hc, a * NT:(a + 1) * NT], W2[:, hc, :], start=(hc == 0), stop=(hc == HC - 1))
                    ins.then_inc(g_psum, 1)
                    if between and a == 0:
                        between()

            def turn_x2(r, b):
                pe.wait_ge(x2_rows, r + 1)
                pe.wait_ge(logits_out, r + 1)
                for a in range(2):
                    for c in range(DC):
                        ins = pe.transpose(bank(7, c * M + a * NT, c * M + (a + 1) * NT), X2now[b][:, a, c * P:(c + 1) * P], ident[0:NT, 0:NT])
                ins.then_inc(x2_turned, 1)

            def router(r, b):
                pe.wait_ge(x2_out, r + 2)
                for a in range(2):
                    for c in range(DC):
                        ins = pe.matmul(bank(7, a * NX, (a + 1) * NX, NT), x2T[b][:, c, a * NT:(a + 1) * NT], gwt[:, c, :],
                                        start=(c == 0), stop=(c == DC - 1))
                ins.then_inc(logits, 1)

            def gnn_step(i, g, b, route_too=True):
                r = 2 * (i - LAG)
                layer1(i, g, b, (lambda: turn_x2(r, 0)) if route_too else None)
                if route_too:
                    router(r, 0)
                if not isinstance(i, int) or i + 1 < MACROS:
                    turn(*after(i, g, b))
                layer2(i, g, b, (lambda: turn_x2(r + 1, 1)) if route_too else None)
                if route_too:
                    router(r + 1, 1)
            turn(0, 0, 0)
            in_pairs(pe, LAG, lambda i, g, b: gnn_step(i, g, b, route_too=False))
            in_pairs(pe, MACROS, gnn_step, ahead=1, first=LAG)
            for r in range(2 * (MACROS - LAG), MACROS):
                turn_x2(r, r % 2)
                router(r, r % 2)

            pe.wait_ge(prefix_in, 1)
            flat = both.rearrange("p e j -> p (e j)")
            for n in range(2):
                pe.matmul(bank(4 + n, 0, EJ // 2, NT), upper, flat[:, n * (EJ // 2):(n + 1) * (EJ // 2)], start=True, stop=True)
            for n in range(2):
                ins = pe.matmul(bank(6 + n, 0, EJ // 2, NT), ones[0:NT, 0:NT], flat[:, n * (EJ // 2):(n + 1) * (EJ // 2)], start=True, stop=True)
            ins.then_inc(prefix_out, 1)
            slots = bank(0, 0, SLOT_TILES)
            pe.matmul(slots, zeros[0:NT, 0:P], ones[0:NT, 0:SLOT_TILES], start=True, stop=False)
            for kk in range(2):
                def place(n, g, b, kk=kk):
                    pe.wait_ge(oh_ready, n + 1 + kk * (TILES // OB))
                    for m in range(OB):
                        ins = pe.matmul(slots, OL[b][:, m, :], OH[b][:, m, :], start=False, stop=False)
                    ins.then_inc(hot_used, 1)
                in_pairs(pe, TILES // OB, place)
            pe.matmul(slots, zeros[0:NT, 0:P], ones[0:NT, 0:SLOT_TILES], start=False, stop=True).then_inc(slots_psum, 1)

            pe.wait_ge(slots_ready, 1)
            pe.wait_ge(texp_ready, 1)
            pe.wait_ge(w_loaded, 2 * NX * 16)

            def turn_slots(i, g, b):
                pe.wait_ge(xg_got[b], (g + 1) * 16)
                pe.wait_ge(xt_ready, i + 1)
                for c in range(DC):
                    ins = pe.transpose(bank(b, c * P, (c + 1) * P), XG[b][:, c * P:(c + 1) * P], ident)
                ins.then_inc(xt_psum, 1)

            def weights(i, at):
                e = pe.value_load(texp[0:1, bass.ds(i, 1)], min_val=0, max_val=NX - 1)
                return lambda off, n: mem[:, bass.ds(e * EW + (ROUTE_END + at + off), n)]

            def expert1(i, g, b):
                w = weights(i, 0)
                pe.wait_ge(xt_ready, i + 3)
                pe.wait_ge(h1_ready, i + 1)
                for c in range(DC):
                    ins = pe.matmul(bank(2 + b), XgT[b][:, c, :], w(c * FF, FF), start=(c == 0), stop=(c == DC - 1))
                ins.then_inc(h1_psum, 1)

            def turn_hidden(i, g, b):
                pe.wait_ge(h1_ready, i + 3)
                pe.wait_ge(h2_ready, i + 1)
                for c in range(FC):
                    ins = pe.transpose(bank(4 + b, c * P, (c + 1) * P), hraw[b][:, c * P:(c + 1) * P], ident)
                ins.then_inc(h2_psum, 1)

            def expert2(i, g, b):
                w = weights(i, DC * FF)
                pe.wait_ge(h2_ready, i + 3)
                pe.wait_ge(y_ready, i + 1)
                for c in range(FC):
                    ins = pe.matmul(bank(6 + b, 0, D), hT[b][:, c, :], w(c * D, D), start=(c == 0), stop=(c == FC - 1))
                ins.then_inc(y_psum, 1)

            def expert_step(i, g, b):
                turn_hidden(i, g, b)
                if not isinstance(i, int) or i + 1 < SLOT_TILES:
                    expert1(*after(i, g, b))
                if not isinstance(i, int) or i + 2 < SLOT_TILES:
                    turn_slots(*after(i, g, b, 2))
                expert2(i, g, b)
            turn_slots(0, 0, 0)
            turn_slots(1, 0, 1)
            expert1(0, 0, 0)
            in_pairs(pe, SLOT_TILES, expert_step, ahead=2)

        @block.vector
        def _(dve):
            for sm, n in ((row_read, 1), (ln_read, 2), (er_read, 2), (c_last, 2)):
                dve.sem_inc(sm, n)
            for sm in (x1b_stored[0], x1b_stored[1], yo_stored[0], yo_stored[1], out_stored[0], out_stored[1],
                       x2_st[0], x2_st[1], st_sum):
                dve.sem_inc(sm, 16)
            st = Steps(dve, dve_setup)

            def op(ins, then=None):
                st.mark(ins)
                st.wait()

            st.mark(dve.memset(Lrow, 0.0))
            dve.wait_ge(ld_dst, 4 * 16)
            dve.tensor_copy(rowF, rowI).then_inc(heads_f, 1)
            st.mark(dve.tensor_copy(tailF, tailI))
            st.wait()
            dve.tensor_tensor(Lrow[:, 1:PIECES], tailF[:, 1:PIECES], tailF[:, 0:PIECES - 1], ALU.is_equal).then_inc(tails_f, 1)

            dve.wait_ge(bc_tails, 1)
            for n, (lo, hi) in enumerate(LINKS):
                st.mark(dve.tensor_copy(L[:, lo:hi], bank(1 + n, 0, hi - lo, 64)))
            st.wait()
            op(dve.tensor_scalar(L[32:64], L[32:64], 2.0, -1.0, ALU.mult, ALU.add))
            op(dve.tensor_scalar(L[32:64], L[32:64], FMAX, None, ALU.mult))
            op(dve.memset(Kk, 1.0))
            op(dve.tensor_tensor(Kk[:, 0:FULL, 1:T], Dst[:, 0:FULL, 1:T], Dst[:, 0:FULL, 0:T - 1], ALU.is_equal))
            op(dve.tensor_tensor(Kk[0:LASTP, FULL, 1:T], Dst[0:LASTP, FULL, 1:T], Dst[0:LASTP, FULL, 0:T - 1], ALU.is_equal))
            op(dve.tensor_scalar(Kx, Kk, 2.0, -1.0, ALU.mult, ALU.add))
            op(dve.tensor_scalar(Kx, Kx, FMAX, None, ALU.mult))
            op(dve.memset(CT[1][0:32], 0.0))
            op(dve.memset(CT[1][32:64], -FMAX))

            def edges(s, g, b):
                parts = LASTP if isinstance(s, int) and s == FULL else P
                now = bass.ds(s, 1)
                dve.wait_ge(e_got[b], (g + 1) * 16)
                dve.wait_ge(st_sum, (s + 1) * 16)
                for f in range(EF):
                    ins = dve.tensor_tensor_scan(out=Sb[0:parts, :, f], data0=Kk[0:parts, now, :].rearrange("p o t -> p (o t)"), data1=Eb[b][0:parts, :, f],
                                                 initial=0.0, op0=ALU.mult, op1=ALU.add)
                ins.then_inc(sum_scanned, 1)
                for f in range(EF):
                    ins = dve.tensor_tensor_scan(out=Eb[b][0:parts, :, f], data0=Kx[0:parts, now, :].rearrange("p o t -> p (o t)"), data1=Eb[b][0:parts, :, f],
                                                 initial=-FMAX, op0=ALU.min, op1=ALU.max)
                ins.then_inc(max_scanned, 1)
                dve.wait_ge(sum_scanned, s + 1)
                dve.wait_ge(max_scanned, s + 1)
                s1 = Steps(dve, carry_step, s * 22)
                for n, rows in enumerate((Sb, Eb[b])):
                    for q in range(4):
                        s1.mark(dve.transpose(CT[b][32 * n:32 * n + 32, :, 32 * q:32 * q + 32],
                                              rows[32 * q:32 * q + 32, T - 1, :].rearrange("p (b c) -> p b c", b=3)))
                s1.wait()
                for n, (mask, o0, o1) in enumerate(((L[0:32], ALU.mult, ALU.add), (L[32:64], ALU.min, ALU.max))):
                    for r in range(3):
                        s1.mark(dve.tensor_tensor_scan(out=CT[b][32 * n:32 * n + 32, r, :], data0=mask[:, bass.ds(s * P, P)], data1=CT[b][32 * n:32 * n + 32, r, :],
                                                       initial=CT[1 - b][32 * n:32 * n + 32, r, P - 1:P], op0=o0, op1=o1))
                s1.wait()
                for n in range(2):
                    for q in range(4):
                        s1.mark(dve.transpose(CR[b][32 * q:32 * q + 32, n, :].rearrange("p (b c) -> p b c", b=3),
                                              CT[b][32 * n:32 * n + 32, :, 32 * q:32 * q + 32]))
                s1.wait()
                assert s1.n == 22
                dve.sem_inc(carry_ready, 1)
            edges(0, 0, 0)

            dve.wait_ge(consts, 1)
            dve.wait_ge(bc_firsts, 1)
            dve.sem_inc(dve_search, 1)
            with dve.Fori(0, TILES) as j:
                dve.wait_ge(dve_search, j + 1)
                dve.scalar_tensor_tensor(out=junk[:, 0:ROWS], in0=bank(0, 0, ROWS, NT), scalar=node[:, bass.ds(j, 1)],
                                         in1=ones[0:NT, 0:ROWS], op0=ALU.is_le, op1=ALU.mult,
                                         accum_out=firsts[:, bass.ds(j, 1)]).then_inc(dve_search, 1)
            dve.wait_ge(dve_search, TILES + 1)
            op(dve.tensor_scalar(firsts, firsts, 1.0, 0.0, ALU.subtract, ALU.max))
            dve.tensor_copy(rowU, firsts).then_inc(rows_ready, 1)

            edges(1, 0, 1)

            def in_row(half):
                dve.wait_ge(row_got, (half + 1) * SB * 16)
                with dve.Fori(0, SB) as m:
                    dve.wait_ge(row_read, m + half * SB + 1)
                    dve.scalar_tensor_tensor(out=junk[:, 0:ROWE], in0=SR[:, bass.ds(m, 1), :].rearrange("p o e -> p (o e)"), scalar=node[:, bass.ds(half * SB + m, 1)],
                                             in1=ones[0:NT, 0:ROWE], op0=ALU.is_le, op1=ALU.mult,
                                             accum_out=inrow[:, bass.ds(half * SB + m, 1)]).then_inc(row_read, 1)
            in_row(0)
            edges(2, 1, 0)
            in_row(1)
            dve.wait_ge(row_read, TILES + 1)
            dve.scalar_tensor_tensor(out=endn, in0=firsts, scalar=float(ROWE), in1=inrow, op0=ALU.mult, op1=ALU.add).then_inc(ends_ready, 1)
            dve.wait_ge(starts_psum, 1)
            op(dve.tensor_copy(startn, bank(5, 0, TILES, NT)))
            op(dve.tensor_tensor(tA, endn, startn, ALU.subtract))
            op(dve.tensor_scalar(has, tA, 1.0, None, ALU.min))
            op(dve.tensor_scalar(tA, tA, 1.0, None, ALU.max))
            op(dve.reciprocal(tB, tA))
            op(dve.tensor_tensor(rch, tB, has, ALU.mult))
            op(dve.tensor_scalar(tA, endn, 1.0, 0.0, ALU.subtract, ALU.max))
            op(dve.tensor_copy(IX[:, :, 0], tA))
            op(dve.tensor_scalar(tB, tA, 1.0 / T, -0.5 + 0.5 / T, ALU.mult, ALU.add))
            op(dve.tensor_scalar(tB, tB, ROUND, None, ALU.add))
            op(dve.tensor_scalar(tB, tB, ROUND, None, ALU.subtract))
            op(dve.tensor_scalar(tA, tB, 1.0, 0.0, ALU.subtract, ALU.max))
            op(dve.tensor_copy(IX[:, :, 1], tA))
            op(dve.tensor_scalar(tB, tB, float(T), None, ALU.mult))
            op(dve.tensor_tensor(cp, startn, tB, ALU.is_lt))
            op(dve.tensor_scalar(cb, cp, 1.0, FMAX, ALU.subtract, ALU.mult))
            op(dve.memset(gatef, float(LEVELS)))
            op(dve.tensor_scalar(gatef[:, 0:MACROS - 1], startn[0:1, 2:TILES:2], 1.0, 0.0, ALU.subtract, ALU.max))
            op(dve.tensor_scalar(gatef[:, 0:MACROS - 1], gatef[:, 0:MACROS - 1], 1.0 / (T * P * LEVEL), 0.5 + 0.5 / (T * P * LEVEL), ALU.mult, ALU.add))
            op(dve.tensor_scalar(gatef, gatef, ROUND, None, ALU.add))
            op(dve.tensor_scalar(gatef, gatef, ROUND, None, ALU.subtract))
            op(dve.tensor_copy(gatei, gatef))
            dve.sem_inc(index_ready, 1)
            dve.wait_ge(cbias_psum, 1)
            dve.tensor_tensor(cbias, bank(4, 0, HC), b1col, ALU.add).then_inc(cbias_ready, 1)
            dve.sem_inc(setup_done, 1)
            edges(3, 1, 1)
            in_pairs(dve, CHUNKS, edges, ahead=2, first=4)

            dve.wait_ge(rstd_ready, 1)
            def norm2(i, g, b):
                s1 = Steps(dve, ln_step, i * 9)
                dve.wait_ge(ln_got[b], (g + 1) * 32)
                dve.wait_ge(x1b_stored[b], (g + 1) * 16)
                for a in range(2):
                    j = bass.ds(2 * i + a, 1)
                    s1.mark(dve.tensor_scalar(Ln[b][:, a, :], Lx[b][:, a, :], rstd[:, j], nmr[:, j], ALU.mult, ALU.add))
                s1.mark(dve.tensor_tensor(Lg[b], Lg[b], b2bc, ALU.add))
                s1.wait()
                s1.mark(dve.tensor_tensor(Lg[b], Lg[b], Ln[b], ALU.add))
                s1.wait()
                s1.mark(dve.tensor_tensor(Lg[b], Lg[b], Lx[b], ALU.add))
                s1.wait()
                for a in range(2):
                    s1.mark(dve.bn_stats(stat[2 * b + a], Lg[b][:, a, :]))
                dve.tensor_tensor(Lb[b], Lg[b], betabc, ALU.add).then_inc(x1b_ready, 1)
                hold(dve, ln_step, i * 9 + s1.n)
                for a in range(2):
                    s1.mark(dve.bn_aggr(mvt2[b][:, a, :], stat[2 * b + a]))
                s1.wait()
                dve.sem_inc(var2_ready, 1)
                assert s1.n == 9

            def norm2_write(i, g, b):
                dve.wait_ge(sd2_ready, i + 1)
                dve.reciprocal(rs_now[b], sd_now[b]).then_inc(rs2_ready, 1)
                dve.wait_ge(rs2_ready, i + 1)
                dve.wait_ge(x2_turned, i + 1)
                dve.wait_ge(x2_st[b], (g + 1) * 16)
                for a in range(2):
                    ins = dve.tensor_scalar(X2now[b][:, a, :], Lg[b][:, a, :], mvt2[b][:, a, 0:1], rs_now[b][:, a:a + 1], ALU.subtract, ALU.mult)
                ins.then_inc(x2_rows, 1)
                dve.wait_ge(x2_rows, i + 1)
                dve.wait_ge(x1b_ready, i + 1)
                dve.sem_inc(ln_read, 1)

            def norm2_step(i, g, b):
                norm2_write(i, g, b)
                if not isinstance(i, int) or i + 2 < MACROS:
                    norm2(*after(i, g, b, 2))
            norm2(0, 0, 0)
            norm2(1, 0, 1)
            in_pairs(dve, MACROS, norm2_step, ahead=2)

            def each_tile(v):
                return spread(v, 1, TILES)

            def each_expert(v):
                return spread(v, 2, NX)

            dve.wait_ge(chunk_done, CHUNKS)
            for e in range(NX):
                st.mark(dve.memset(ioe[:, :, e:e + 1], float(NX - e)))
            st.mark(dve.memset(keepm, 1.0))
            st.wait()
            op(dve.memset(keepm[:, :, 0:1], 0.0))

            dve.wait_ge(logits_out, MACROS + 1)
            op(dve.tensor_tensor(Lo, Lo, each_tile(gbbc), ALU.add))

            def top(O, at):
                op(dve.tensor_reduce(at, Lo, AX_X, ALU.max))
                op(dve.tensor_tensor(Rk, Lo, each_expert(at), ALU.is_equal))
                op(dve.tensor_tensor(Rk, Rk, ioe, ALU.mult))
                op(dve.tensor_reduce(tA, Rk, AX_X, ALU.max))
                op(dve.tensor_tensor(O, Rk, each_expert(tA), ALU.is_equal))
            top(Oa, v0[:, 0, :])
            op(dve.scalar_tensor_tensor(out=Lo.rearrange("p j e -> p (j e)"), in0=Oa.rearrange("p j e -> p (j e)"), scalar=-3.0e38,
                                        in1=Lo.rearrange("p j e -> p (j e)"), op0=ALU.mult, op1=ALU.add))
            top(Ob, v0[:, 1, :])
            dve.tensor_tensor(both.rearrange("p e j -> p j e"), Oa, Ob, ALU.add).then_inc(prefix_in, 1)
            dve.tensor_tensor(v0[:, 0, :], v0[:, 1, :], v0[:, 0, :], ALU.subtract).then_inc(gap_ready, 1)
            dve.wait_ge(prefix_out, 1)
            op(dve.tensor_copy(tot.rearrange("p e j -> p (e j)")[:, 0:EJ // 2], bank(6, 0, EJ // 2, NT)))
            op(dve.tensor_copy(tot.rearrange("p e j -> p (e j)")[:, EJ // 2:EJ], bank(7, 0, EJ // 2, NT)))
            op(dve.tensor_tensor_scan(out=incl.rearrange("p e j -> p (e j)"), data0=keepm.rearrange("p e j -> p (e j)"),
                                      data1=tot.rearrange("p e j -> p (e j)"), initial=0.0, op0=ALU.mult, op1=ALU.add))
            op(dve.tensor_scalar(eN, incl[:, :, TILES - 1], 1.0 / P, 0.5 - 0.5 / P, ALU.mult, ALU.add))
            op(dve.tensor_scalar(eN, eN, ROUND, None, ALU.add))
            op(dve.tensor_scalar(eN, eN, ROUND, None, ALU.subtract))
            op(dve.tensor_tensor_scan(out=eI, data0=ones[0:NT, 0:NX], data1=eN, initial=0.0, op0=ALU.mult, op1=ALU.add))
            op(dve.tensor_tensor(eE, eI, eN, ALU.subtract))
            op(dve.tensor_scalar(eE, eE, float(P), None, ALU.mult))
            op(dve.tensor_tensor(tcmp, spread(eI[0:1], 1, SLOT_TILES), spread(numbers[0:1, 0:SLOT_TILES], 2, NX), ALU.is_le))
            op(dve.tensor_reduce(tsum, tcmp, AX_X, ALU.add))
            op(dve.tensor_scalar(tsum, tsum, float(NX - 1), None, ALU.min))
            dve.tensor_copy(texp, tsum).then_inc(texp_ready, 1)
            op(dve.tensor_tensor(incl, incl, tot, ALU.subtract))
            for n in range(2):
                op(dve.tensor_tensor(incl[:, n * NX // 2:(n + 1) * NX // 2, :], incl[:, n * NX // 2:(n + 1) * NX // 2, :],
                                     bank(4 + n, 0, EJ // 2, NT).rearrange("p (e j) -> p e j", j=TILES), ALU.add))
            op(dve.tensor_tensor(incl, incl, spread(eE, 2, TILES), ALU.add))
            for kk, O in enumerate((Oa, Ob)):
                op(dve.tensor_tensor(Rk, O, incl.rearrange("p e j -> p j e"), ALU.mult))
                op(dve.tensor_reduce(loq[:, kk, :], Rk, AX_X, ALU.add))
            flat2 = "p k j -> p (k j)"
            op(dve.tensor_copy(posU, loq))
            op(dve.tensor_scalar(hiq, loq, 1.0 / P, -0.5 + 0.5 / P, ALU.mult, ALU.add))
            op(dve.tensor_scalar(hiq, hiq, ROUND, None, ALU.add))
            op(dve.tensor_scalar(hiq, hiq, ROUND, None, ALU.subtract))
            op(dve.scalar_tensor_tensor(out=loq.rearrange(flat2), in0=hiq.rearrange(flat2), scalar=-float(P), in1=loq.rearrange(flat2), op0=ALU.mult, op1=ALU.add))
            for kk in range(2):
                def hi_rows(n, g, b, kk=kk):
                    dve.wait_ge(hot_used, n + 1 + kk * (TILES // OB))
                    dve.tensor_tensor(OL[b], spread(numbers[0:NT], 1, OB), spread(loq[:, kk, bass.ds(n * OB, OB)], 2, P), ALU.is_equal)
                    for m in range(OB):
                        j = bass.ds(n * OB + m, 1)
                        ins = dve.scalar_tensor_tensor(out=OH[b][:, m, :], in0=numbers[0:NT, 0:SLOT_TILES], scalar=hiq[:, kk, j],
                                                       in1=node[:, j].to_broadcast([NT, SLOT_TILES]), op0=ALU.is_equal, op1=ALU.mult)
                    ins.then_inc(oh_ready, 1)
                in_pairs(dve, TILES // OB, hi_rows)
            dve.wait_ge(slots_psum, 1)
            dve.tensor_copy(slotU, bank(0, 0, SLOT_TILES)).then_inc(slots_ready, 1)
            dve.wait_ge(e_gap, 1)
            op(dve.tensor_scalar(tB, v0[:, 1, :], 1.0, None, ALU.add))
            op(dve.reciprocal(wsel[:, 0, :], tB))
            op(dve.tensor_tensor(wsel[:, 1, :], wsel[:, 0, :], v0[:, 1, :], ALU.mult))
            dve.sem_inc(dve_free, 1)

            def take_slots(i, g, b):
                dve.wait_ge(xt_psum, i + 3)
                dve.tensor_copy(XgT[b].rearrange("p c n -> p (c n)"), bank(b, 0, DC * P)).then_inc(xt_ready, 1)

            def take_hidden(i, g, b):
                dve.wait_ge(h1_psum, i + 1)
                dve.tensor_copy(hraw[b], bank(2 + b)).then_inc(h1_ready, 1)

            def take_y(i, g, b):
                e = dve.value_load(texp[0:1, bass.ds(i, 1)], min_val=0, max_val=NX - 1)
                dve.wait_ge(y_psum, i + 3)
                dve.wait_ge(yo_stored[b], (g + 1) * 16)
                dve.tensor_tensor(YO[b], bank(6 + b, 0, D), eb2bc[:, bass.ds(e, 1), :].rearrange("p o d -> p (o d)"), ALU.add).then_inc(y_ready, 1)

            def expert_step(i, g, b):
                if not isinstance(i, int) or i + 1 < SLOT_TILES:
                    take_hidden(*after(i, g, b))
                if not isinstance(i, int) or i + 2 < SLOT_TILES:
                    take_slots(*after(i, g, b, 2))
                take_y(i, g, b)
            dve.wait_ge(eb2_loaded, 16)
            take_slots(0, 0, 0)
            take_slots(1, 0, 1)
            take_hidden(0, 0, 0)
            in_pairs(dve, SLOT_TILES, expert_step, ahead=2)

            def combine(i, g, b):
                s1 = Steps(dve, c_step, i * (4 * CB + 2))
                dve.wait_ge(ex_got[b], (g + 1) * 16)
                dve.wait_ge(er_got[b], (g + 1) * 2 * CB * 16)
                for kk, (before, after_) in enumerate(((EX[b], Y1[b]), (Y1[b], Y2[b]))):
                    for m in range(CB):
                        s1.mark(dve.scalar_tensor_tensor(out=after_[:, m, :], in0=ER[b][:, kk, m, :], scalar=wsel[:, kk, bass.ds(i * CB + m, 1)],
                                                         in1=before[:, m, :], op0=ALU.mult, op1=ALU.add))
                    hold(dve, c_step, i * (4 * CB + 2) + s1.n)
                dve.sem_inc(er_read, 1)
                for m in range(CB):
                    s1.mark(dve.bn_stats(statc[b][:, m, :], Y2[b][:, m, :]))
                hold(dve, c_step, i * (4 * CB + 2) + s1.n)
                for m in range(CB):
                    s1.mark(dve.bn_aggr(mvc[b][:, m, :], statc[b][:, m, :]))
                s1.wait()
                dve.sem_inc(c_var, 1)
                dve.wait_ge(c_sd, i + 1)
                s1.mark(dve.reciprocal(rsc[b], sdc[b]))
                s1.wait()
                s1.mark(dve.scalar_tensor_tensor(out=nmc[b], in0=mvc[b][:, :, 0], scalar=-1.0, in1=rsc[b], op0=ALU.mult, op1=ALU.mult))
                s1.wait()
                dve.sem_inc(c_nm, 1)
                assert s1.n == 4 * CB + 2

            def finish(i, g, b):
                dve.wait_ge(c_norm, i + 1)
                dve.wait_ge(out_stored[b], (g + 1) * 16)
                dve.tensor_tensor(Y4[b], Y3[b], spread(gammabc, 1, CB), ALU.mult).then_inc(c_last, 1)
                dve.wait_ge(c_last, i + 3)
                dve.wait_ge(eb_got[b], (g + 1) * 16)
                dve.tensor_tensor(Y4[b], Y4[b], EB[b], ALU.add).then_inc(c_out, 1)

            def combine_step(i, g, b):
                if not isinstance(i, int) or i + 1 < TILES // CB:
                    combine(*after(i, g, b))
                finish(i, g, b)
            combine(0, 0, 0)
            in_pairs(dve, TILES // CB, combine_step, ahead=1)


_INS = ['x', 'dst', 'edge_attr_96', 'L0_gnn_u', 'L0_gnn_W1', 'L0_gnn_b1', 'L0_gnn_W2', 'L0_gnn_b2', 'L0_ffn_gate_w',
        'L0_ffn_gate_b', 'L0_ffn_w1', 'L0_ffn_b1', 'L0_ffn_w2', 'L0_ffn_b2', 'L0_ffn_gamma', 'L0_ffn_beta']
_OUTS = [((6250, 256), 'float32')]


def kernel(**inputs):
    import numpy as _np
    import concourse.bacc as _bacc
    from concourse import mybir as _mybir
    from concourse.bass_utils import run_bass_kernel_spmd as _run

    nc = _bacc.Bacc("TRN2", target_bir_lowering=False, num_devices=1)
    arrays, args = {}, []
    for name in _INS:
        a = _np.ascontiguousarray(inputs[name])
        arrays[f"in_{name}_dram"] = a
        args.append(nc.dram_tensor(f"in_{name}_dram", a.shape, _mybir.dt.from_np(a.dtype), kind="ExternalInput").ap())
    for i, (shape, dtype) in enumerate(_OUTS):
        dt = _mybir.dt.from_np(_np.dtype(dtype))
        args.append(nc.dram_tensor(f"out_{i}_dram", shape, dt, kind="ExternalOutput").ap())
    gnn_moe_kernel(nc, *args)
    r = _run(nc, [arrays], core_ids=[0])
    got = tuple(r.results[0][f"out_{i}_dram"] for i in range(len(_OUTS)))
    return got[0]
```
